# Optimizing a Trainium2 kernel written in Bass

```python
import numpy as np
import jax
import jax.numpy as jnp

def _softmax(x, axis=-1):
    return jax.nn.softmax(x, axis=axis)

def _gelu(x):
    return jax.nn.gelu(x, approximate=True)

def _silu(x):
    return jax.nn.silu(x)

def _sigmoid(x):
    return jax.nn.sigmoid(x)

def _layernorm(x, axis=-1, eps=1e-05):
    m = jnp.mean(x, axis=axis, keepdims=True)
    v = jnp.var(x, axis=axis, keepdims=True)
    return (x - m) / jnp.sqrt(v + eps)

def _scatter_add(tgt, idx, src, axis=0):
    return tgt.at[idx].add(src)

def _segment_sum(src, seg, n):
    return jax.ops.segment_sum(src, seg, n)
kernel_name = 'mk_adaln_ffn_d1_seqx_r4_8850f1'

def setup_inputs(seed: int=0):
    np.random.seed(seed)
    _w = jnp.asarray

    def _rec_inputs():
        import jax
        import jax.numpy as jnp
        _rk = jax.random.key(seed)
        x = -0.000125 + 0.9999 * jax.random.normal(jax.random.fold_in(_rk, 1), (64, 64, 256), jnp.float32)
        _lenS = 64 - jax.random.randint(jax.random.fold_in(_rk, 7), (64,), 0, max(1, 64 // 4) + 1, jnp.int32)
        _lenS2 = 64 - jax.random.randint(jax.random.fold_in(_rk, 8), (64,), 0, max(1, 64 // 4) + 1, jnp.int32)
        itok_B_0_30 = jax.random.randint(jax.random.fold_in(_rk, 11), (64,), 0, 31, jnp.int32)
        return (x, itok_B_0_30)
    x, itok_B_0_30 = _rec_inputs()

    def _L0_cond_setup():
        import jax, jax.numpy as jnp
        import numpy as np
        C, I, O = (32, 256, 256)
        B, T = (64, 128)
        key = jax.random.key(seed)
        kx, kc, kw, kb = jax.random.split(key, 4)
        x = jax.random.normal(kx, (B, T, I), dtype=jnp.float32)
        cat_ids = jax.random.randint(kc, (B,), 0, C)
        W = 0.02 * jax.random.normal(kw, (C, I, O), dtype=jnp.float32)
        b = jnp.zeros((C, O), dtype=jnp.float32)
        return {'x': x, 'cat_ids': cat_ids, 'W': W, 'b': b}
    _L0_cond_all = _L0_cond_setup()
    _L0_cond_in = {k: v for k, v in _L0_cond_all.items() if k in ('W', 'b')}
    del _L0_cond_all

    def _L0_ffn_setup():
        import jax, jax.numpy as jnp
        import numpy as np
        key = jax.random.key(seed)
        k1, k2, k3 = jax.random.split(key, 3)
        B, T, D, E = (4, 512, 256, 8)
        x = jax.random.normal(k1, (B, T, D), dtype=jnp.float32)
        gate_w = jax.random.normal(k2, (E, D), dtype=jnp.float32) * (1.0 / np.sqrt(D))
        bound = float(np.sqrt(6.0 / (D + D)))
        We = jax.random.uniform(k3, (E, D, D), dtype=jnp.float32, minval=-bound, maxval=bound)
        return {'x': x, 'gate_w': gate_w, 'We': We}
    _L0_ffn_all = _L0_ffn_setup()
    _L0_ffn_in = {k: v for k, v in _L0_ffn_all.items() if k in ('gate_w', 'We')}
    del _L0_ffn_all
    return {'x': x, 'itok_B_0_30': itok_B_0_30, 'L0_cond_W': _L0_cond_in['W'], 'L0_cond_b': _L0_cond_in['b'], 'L0_ffn_gate_w': _L0_ffn_in['gate_w'], 'L0_ffn_We': _L0_ffn_in['We']}

def reference(x, itok_B_0_30, L0_cond_W, L0_cond_b, L0_ffn_gate_w, L0_ffn_We):
    import jax
    import jax.numpy as jnp

    def _L0_cond_ref(x, cat_ids, W, b):
        import jax, jax.numpy as jnp
        import numpy as np
        C, I, O = (32, 256, 256)
        B, T = (64, 128)
        selected_W = W[cat_ids]
        selected_b = b[cat_ids]
        if x.ndim == 2:
            return jnp.einsum('bi,bio->bo', x, selected_W) + selected_b
        return jnp.einsum('bti,bio->bto', x, selected_W) + selected_b[:, None, :]

    def _L0_ffn_ref(x, gate_w, We):
        import jax, jax.numpy as jnp
        import numpy as np
        top_k = 2
        logits = jnp.einsum('btd,ed->bte', x, gate_w)
        top_val, top_idx = jax.lax.top_k(logits, top_k)
        top_w = jax.nn.softmax(top_val, axis=-1)
        y_all = jnp.einsum('btd,edm->btem', x, We)
        x_experts = jnp.take_along_axis(y_all, top_idx[..., None], axis=2)
        out = jnp.sum(x_experts * top_w[..., None], axis=2)
        return out
    x = x + _L0_ffn_ref(_L0_cond_ref(x, itok_B_0_30, L0_cond_W, L0_cond_b), L0_ffn_gate_w, L0_ffn_We)
    return x

_drawn_inputs = setup_inputs


def setup_inputs(seed=0):
    import zlib

    import numpy as np

    out = dict(_drawn_inputs(seed))
    spreads = {'L0_cond_b': (0.0, 0.1)}
    factors = {}
    for name, (base, spread) in spreads.items():
        noise = np.random.default_rng([zlib.crc32(name.encode()), seed]).standard_normal(out[name].shape)
        drawn = base * np.exp(spread * noise) if base else spread * noise
        out[name] = jnp.asarray(drawn.astype(out[name].dtype))
    for name, factor in factors.items():
        out[name] = (out[name] * factor).astype(out[name].dtype)
    return out
```

```python
from contextlib import ExitStack

import concourse.bass as bass
from concourse import mybir

F32 = mybir.dt.float32
F32R = mybir.dt.float32r
I32 = mybir.dt.int32
U32 = mybir.dt.uint32
ALU = mybir.AluOpType
ACT = mybir.ActivationFunctionType

P = 128
RING = 4


def build(nc, x, cat, W, bias, gate, We, out):
    B, T, D = x.shape
    C = W.shape[0]
    E = We.shape[0]
    K = D // P
    BT = P // T
    TILES = B * T // P
    BANKS = E // 2
    M = 2 * D
    assert K * P == D and BT * T == P and TILES % RING == 0 and M == 512

    x_t = x.rearrange("b t d -> (b t) d").rearrange("(n p) d -> n p d", p=P)
    out_t = out.rearrange("b t d -> (b t) d").rearrange("(n p) d -> n p d", p=P)

    ctx = ExitStack()
    with ctx:
        def sb(name, shape, dt=F32):
            return ctx.enter_context(nc.sbuf_tensor(name, shape, dt))

        def pb(name, shape, dt=F32):
            return ctx.enter_context(nc.psum_tensor(name, shape, dt))

        def sem(name):
            return ctx.enter_context(nc.semaphore(name))

        ident = sb("ident", [P, P])
        iota_e = sb("iota_e", [P, E])
        iota_c = sb("iota_c", [C, 1])
        cats = sb("cats", [1, B], I32)
        cats_all = sb("cats_all", [C, B], I32)
        cats_f = sb("cats_f", [C, B])
        onehot_c = sb("onehot_c", [C, B])
        bias_sb = sb("bias_sb", [C, D])
        bias_t = sb("bias_t", [P, K, B])
        gate_sb = sb("gate_sb", [E, D])
        gate_f = sb("gate_f", [P, K, E])
        gate_hl = sb("gate_hl", [P, K, 2, E], F32R)
        we_f = sb("we_f", [P, K, E * D])
        we_hi = sb("we_hi", [P, K, E * D], F32R)
        we_lo = sb("we_lo", [P, K, E * D], F32R)
        x_sb = sb("x_sb", [P, RING, D])
        w_sb = sb("w_sb", [P, RING, BT, K, D])
        w_hi = sb("w_hi", [P, 2, BT, K, D], F32R)
        w_lo = sb("w_lo", [P, 2, BT, K, D], F32R)
        xt = sb("xt", [P, 2, K, BT, 2, T], F32R)
        h_low = sb("h_low", [P, 2, K, BT, T])
        h_bias = sb("h_bias", [P, 2, K, BT, T])
        h_f = sb("h_f", [P, 2, K, BT, T])
        h_hi = sb("h_hi", [P, 2, K, P], F32R)
        h_lo = sb("h_lo", [P, 2, K, P], F32R)
        lg2 = sb("lg2", [P, 2, 2, E])
        lg = sb("lg", [P, 2, E])
        top = sb("top", [P, 2, 8])
        topi = sb("topi", [P, 2, 8], U32)
        topf = sb("topf", [P, 2, 2])
        ex = sb("ex", [P, 2, 1])
        den = sb("den", [P, 2, 1])
        w1 = sb("w1", [P, 2, 1])
        w2 = sb("w2", [P, 2, 1])
        wt1 = sb("wt1", [P, 2, E])
        wt2 = sb("wt2", [P, 2, E])
        wt = sb("wt", [P, 2, E])
        acc = sb("acc", [P, 2, 2, D])

        ps_turn = pb("ps_turn", [P, K, P])
        ps_cond = pb("ps_cond", [P, K, BT, 2, T])
        ps_gate = pb("ps_gate", [P, 512])
        ps_exp = [pb(f"ps_exp{j}", [P, M]) for j in range(BANKS)]

        small_in = sem("small_in")
        x_in = [sem(f"x_in{j}") for j in range(RING)]
        w_in = [sem(f"w_in{j}") for j in range(RING)]
        we_in = [sem(f"we_in{j}") for j in range(BANKS)]
        filled = sem("filled")
        ident_ok = sem("ident_ok")
        catsf_ok = sem("catsf_ok")
        onehot_ok = sem("onehot_ok")
        pre_pe = sem("pre_pe")
        pre_copied = sem("pre_copied")
        gatehi_ok = sem("gatehi_ok")
        gatelo_ok = sem("gatelo_ok")
        wehi_ok = sem("wehi_ok")
        welo_ok = sem("welo_ok")
        turned = sem("turned")
        xhi_ok = sem("xhi_ok")
        xlo_ok = sem("xlo_ok")
        whi_ok = sem("whi_ok")
        wlo_ok = sem("wlo_ok")
        conded = sem("conded")
        hlow_ok = sem("hlow_ok")
        hbias_ok = sem("hbias_ok")
        hf_ok = sem("hf_ok")
        hhi_ok = sem("hhi_ok")
        hlo_ok = sem("hlo_ok")
        gated = sem("gated")
        lg2_ok = sem("lg2_ok")
        lg_ok = sem("lg_ok")
        top_ok = sem("top_ok")
        topi_ok = sem("topi_ok")
        topf_ok = sem("topf_ok")
        ex_ok = sem("ex_ok")
        den_ok = sem("den_ok")
        w1_ok = sem("w1_ok")
        w2_ok = sem("w2_ok")
        wt12_ok = sem("wt12_ok")
        wt_ok = sem("wt_ok")
        banked = sem("banked")
        added = sem("added")
        stored = [sem(f"stored{j}") for j in range(2)]

        block = ctx.enter_context(nc.Block())

        def tiles(eng, step):
            for j in range(RING):
                step(j, j)
            with eng.Fori(1, TILES // RING - 1) as i:
                for j in range(RING):
                    step(i * RING + j, j)
            for j in range(RING):
                step(TILES - RING + j, j)

        def is_past(u, n):
            return not isinstance(u, int) or u >= n

        def is_within(u, n):
            return not isinstance(u, int) or u + n < TILES

        @block.sync
        def _(sp):
            sp.dma_start(cats[:], cat.rearrange("(a b) -> a b", a=1)).then_inc(small_in, 16)
            sp.dma_start(x_sb[:, 0, :], x_t[0]).then_inc(x_in[0], 16)
            sp.dma_start(x_sb[:, 1, :], x_t[1]).then_inc(x_in[1], 16)

            def load_w(u, j):
                for b in range(BT):
                    c = sp.value_load(cats[0:1, bass.ds(u * BT + b, 1)], min_val=0, max_val=C - 1)
                    sp.dma_start(w_sb[:, j, b], W[bass.ds(c, 1)].rearrange("a (k p) o -> p (a k) o", p=P)
                                 ).then_inc(w_in[j], 16)

            sp.wait_ge(small_in, 16 * 4)
            load_w(0, 0)
            load_w(1, 1)
            for n in range(BANKS):
                for e in (2 * n, 2 * n + 1):
                    sp.dma_start(we_f[:, :, e * D:(e + 1) * D], We[e].rearrange("(k p) m -> p k m", p=P)
                                 ).then_inc(we_in[n], 16)
                if n < 2:
                    sp.dma_start(x_sb[:, 2 + n, :], x_t[2 + n]).then_inc(x_in[2 + n], 16)
                    load_w(2 + n, 2 + n)

            def step(u, j):
                if is_within(u, RING):
                    sp.wait_ge(whi_ok, u + 1)
                    sp.wait_ge(wlo_ok, u + 1)
                    load_w(u + RING, j)
                sp.wait_ge(added, (u + 1) * E)
                sp.dma_start(out_t[bass.ds(u, 1)].rearrange("a p d -> p (a d)"), acc[:, j % 2, 1, :]
                             ).then_inc(stored[j % 2], 16)
                if is_within(u, RING):
                    sp.dma_start(x_sb[:, j, :], x_t[bass.ds(u + RING, 1)].rearrange("a p d -> p (a d)")
                                 ).then_inc(x_in[j], 16)

            tiles(sp, step)
            for j in range(2):
                sp.wait_ge(stored[j], 16 * TILES // 2)

        @block.gpsimd
        def _(pool):
            nc.gpsimd.memset(ident[:], 0.0).then_inc(filled, 1)
            nc.gpsimd.iota(iota_e[:], pattern=[[1, E]], base=0, channel_multiplier=0,
                           allow_small_or_imprecise_dtypes=True).then_inc(filled, 1)
            nc.gpsimd.iota(iota_c[:], pattern=[[0, 1]], base=0, channel_multiplier=1,
                           allow_small_or_imprecise_dtypes=True).then_inc(filled, 1)
            pool.wait_ge(filled, 3)
            nc.gpsimd.affine_select(out=ident[:], in_=ident[:], compare_op=ALU.not_equal, fill=1.0, base=0,
                                    pattern=[[-1, P]], channel_multiplier=1).then_inc(ident_ok, 1)

            def split_w(u, j):
                pool.wait_ge(whi_ok, u + 1)
                if is_past(u, 2):
                    pool.wait_ge(conded, u - 1)
                nc.gpsimd.tensor_tensor(w_lo[:, j % 2], w_sb[:, j], w_hi[:, j % 2].bitcast(F32),
                                        ALU.subtract).then_inc(wlo_ok, 1)

            def add_bias(u, j):
                pool.wait_ge(hlow_ok, u + 1)
                if not is_past(u, 1):
                    pool.wait_ge(pre_copied, 2)
                nc.gpsimd.tensor_tensor(h_bias[:, j % 2], h_low[:, j % 2],
                                        bias_t[:, :, bass.ds(u * BT, BT)].unsqueeze(3).to_broadcast([P, K, BT, T]),
                                        ALU.add).then_inc(hbias_ok, 1)

            def split_h(u, j):
                pool.wait_ge(hhi_ok, u + 1)
                if is_past(u, 2):
                    pool.wait_ge(banked, (u - 1) * BANKS)
                nc.gpsimd.tensor_tensor(h_lo[:, j % 2], h_f[:, j % 2].rearrange("p k b t -> p k (b t)"),
                                        h_hi[:, j % 2].bitcast(F32), ALU.subtract).then_inc(hlo_ok, 1)

            split_w(0, 0)
            split_w(1, 1)
            add_bias(0, 0)
            split_h(0, 0)

            def step(u, j):
                if is_within(u, 1):
                    add_bias(u + 1, (j + 1) % RING)
                    split_h(u + 1, (j + 1) % RING)
                if is_within(u, 2):
                    split_w(u + 2, (j + 2) % RING)

            tiles(pool, step)

        @block.scalar
        def _(act):
            act.dma_start(cats_all[:], cat.partition_broadcast(C)).then_inc(small_in, 16)
            act.dma_start(bias_sb[:], bias).then_inc(small_in, 16)
            act.dma_start(gate_sb[:], gate).then_inc(small_in, 16)

            def turn_hi(u, j):
                act.wait_ge(turned, u + 1)
                if is_past(u, 2):
                    act.wait_ge(conded, u - 1)
                nc.scalar.activation(xt[:, j % 2, :, :, 0, :], ps_turn[:].rearrange("p k (b t) -> p k b t", b=BT),
                                     ACT.Copy).then_inc(xhi_ok, 1)

            def w_high(u, j):
                act.wait_ge(w_in[j], (u // RING + 1) * 16 * BT if isinstance(u, int) else (u - j) * (16 * BT // RING) + 16 * BT)
                if is_past(u, 2):
                    act.wait_ge(conded, u - 1)
                    act.wait_ge(wlo_ok, u - 1)
                nc.scalar.activation(w_hi[:, j % 2], w_sb[:, j], ACT.Copy).then_inc(whi_ok, 1)

            def cond_low(u, j):
                act.wait_ge(conded, u + 1)
                if is_past(u, 2):
                    act.wait_ge(hbias_ok, u - 1)
                nc.scalar.activation(h_low[:, j % 2], ps_cond[:, :, :, 1, :], ACT.Copy).then_inc(hlow_ok, 1)

            def h_high(u, j):
                act.wait_ge(hf_ok, u + 1)
                if is_past(u, 2):
                    act.wait_ge(banked, (u - 1) * BANKS)
                    act.wait_ge(hlo_ok, u - 1)
                nc.scalar.activation(h_hi[:, j % 2], h_f[:, j % 2].rearrange("p k b t -> p k (b t)"),
                                     ACT.Copy).then_inc(hhi_ok, 1)

            act.wait_ge(pre_pe, 1)
            nc.scalar.activation(gate_f[:], ps_gate[:, 0:K * E].rearrange("p (k e) -> p k e", k=K),
                                 ACT.Copy).then_inc(pre_copied, 1)
            act.wait_ge(pre_copied, 1)
            nc.scalar.activation(gate_hl[:, :, 0, :], gate_f[:], ACT.Copy).then_inc(gatehi_ok, 1)
            turn_hi(0, 0)
            w_high(0, 0)
            act.wait_ge(pre_pe, 2)
            nc.scalar.activation(bias_t[:], ps_exp[0][:, 0:K * B].rearrange("p (k b) -> p k b", k=K),
                                 ACT.Copy).then_inc(pre_copied, 1)
            turn_hi(1, 1)
            w_high(1, 1)
            cond_low(0, 0)
            h_high(0, 0)
            for n in range(BANKS):
                act.wait_ge(we_in[n], 32)
                nc.scalar.activation(we_hi[:, :, n * M:(n + 1) * M], we_f[:, :, n * M:(n + 1) * M],
                                     ACT.Copy).then_inc(wehi_ok, 1)

            def step(u, j):
                act.wait_ge(gated, u + 1)
                if is_past(u, 2):
                    act.wait_ge(lg_ok, u - 1)
                nc.scalar.activation(lg2[:, j % 2], ps_gate[:, 0:2 * E].rearrange("p (s e) -> p s e", s=2),
                                     ACT.Copy).then_inc(lg2_ok, 1)
                if is_within(u, 1):
                    cond_low(u + 1, (j + 1) % RING)
                act.wait_ge(top_ok, u + 1)
                if is_past(u, 2):
                    act.wait_ge(w2_ok, u - 1)
                nc.scalar.activation(ex[:, j % 2], top[:, j % 2, 0:1], ACT.Exp, bias=top[:, j % 2, 1:2],
                                     scale=-1.0).then_inc(ex_ok, 1)
                if is_within(u, 2):
                    turn_hi(u + 2, (j + 2) % RING)
                if is_within(u, 1):
                    h_high(u + 1, (j + 1) % RING)
                if is_within(u, 2):
                    w_high(u + 2, (j + 2) % RING)

            tiles(act, step)

        @block.vector
        def _(dve):
            dve.wait_ge(small_in, 16 * 4)
            nc.vector.tensor_copy(cats_f[:], cats_all[:]).then_inc(catsf_ok, 1)
            dve.wait_ge(catsf_ok, 1)
            dve.wait_ge(filled, 3)
            nc.vector.tensor_scalar(onehot_c[:], cats_f[:], iota_c[:, 0:1], None, ALU.is_equal).then_inc(onehot_ok, 1)
            dve.wait_ge(gatehi_ok, 1)
            nc.vector.tensor_tensor(gate_hl[:, :, 1, :], gate_f[:], gate_hl[:, :, 0, :].bitcast(F32),
                                    ALU.subtract).then_inc(gatelo_ok, 1)

            def turn_lo(u, j):
                dve.wait_ge(xhi_ok, u + 1)
                nc.vector.tensor_tensor(xt[:, j % 2, :, :, 1, :], ps_turn[:].rearrange("p k (b t) -> p k b t", b=BT),
                                        xt[:, j % 2, :, :, 0, :].bitcast(F32), ALU.subtract).then_inc(xlo_ok, 1)

            def cond_sum(u, j):
                dve.wait_ge(hbias_ok, u + 1)
                if is_past(u, 2):
                    dve.wait_ge(hlo_ok, u - 1)
                nc.vector.tensor_tensor(h_f[:, j % 2], ps_cond[:, :, :, 0, :], h_bias[:, j % 2],
                                        ALU.add).then_inc(hf_ok, 1)

            turn_lo(0, 0)
            turn_lo(1, 1)
            cond_sum(0, 0)
            for n in range(BANKS):
                dve.wait_ge(wehi_ok, n + 1)
                nc.vector.tensor_tensor(we_lo[:, :, n * M:(n + 1) * M], we_f[:, :, n * M:(n + 1) * M],
                                        we_hi[:, :, n * M:(n + 1) * M].bitcast(F32), ALU.subtract).then_inc(welo_ok, 1)

            def step(u, j):
                s = j % 2
                if is_past(u, 2):
                    dve.wait_ge(ex_ok, u - 1)
                dve.wait_ge(lg2_ok, u + 1)
                nc.vector.tensor_tensor(lg[:, s], lg2[:, s, 0], lg2[:, s, 1], ALU.add).then_inc(lg_ok, 1)
                dve.wait_ge(filled, 3)
                dve.wait_ge(lg_ok, u + 1)
                nc.vector.max(top[:, s], lg[:, s]).then_inc(top_ok, 1)
                dve.wait_ge(filled, 3)
                dve.wait_ge(top_ok, u + 1)
                nc.vector.max_index(topi[:, s], top[:, s], lg[:, s]).then_inc(topi_ok, 1)
                dve.wait_ge(topi_ok, u + 1)
                nc.vector.tensor_copy(topf[:, s], topi[:, s, 0:2]).then_inc(topf_ok, 1)
                dve.wait_ge(ex_ok, u + 1)
                nc.vector.tensor_scalar_add(den[:, s], ex[:, s], 1.0).then_inc(den_ok, 1)
                dve.wait_ge(den_ok, u + 1)
                nc.vector.reciprocal(w1[:, s], den[:, s]).then_inc(w1_ok, 1)
                dve.wait_ge(w1_ok, u + 1)
                nc.vector.tensor_tensor(w2[:, s], ex[:, s], w1[:, s], ALU.mult).then_inc(w2_ok, 1)
                dve.wait_ge(w2_ok, u + 1)
                dve.wait_ge(topf_ok, u + 1)
                for wtn, wn, n in ((wt1, w1, 0), (wt2, w2, 1)):
                    nc.vector.tensor_scalar(wtn[:, s], iota_e[:], topf[:, s, n:n + 1], wn[:, s],
                                            ALU.is_equal, ALU.mult).then_inc(wt12_ok, 1)
                dve.wait_ge(wt12_ok, 2 * (u + 1))
                nc.vector.tensor_tensor(wt[:, s], wt1[:, s], wt2[:, s], ALU.add).then_inc(wt_ok, 1)
                dve.wait_ge(wt_ok, u + 1)
                if is_within(u, 1):
                    cond_sum(u + 1, (j + 1) % RING)
                if is_within(u, 2):
                    turn_lo(u + 2, (j + 2) % RING)
                if is_past(u, 2):
                    dve.wait_ge(stored[s], (u - j) * 8 + (j // 2) * 16)
                for e in range(E):
                    if e % 2 == 0:
                        dve.wait_ge(banked, u * BANKS + e // 2 + 1)
                    if e:
                        dve.wait_ge(added, u * E + e)
                    before = x_sb[:, j, :] if e == 0 else acc[:, s, (e + 1) % 2 , :]
                    nc.vector.scalar_tensor_tensor(
                        out=acc[:, s, e % 2, :], in0=ps_exp[e // 2][:, (e % 2) * D:(e % 2 + 1) * D],
                        scalar=wt[:, s, e:e + 1], in1=before, op0=ALU.mult, op1=ALU.add).then_inc(added, 1)

            tiles(dve, step)

        @block.tensor
        def _(pe):
            pe.wait_ge(small_in, 16 * 4)
            pe.wait_ge(ident_ok, 1)
            for k in range(K):
                last = nc.tensor.transpose(ps_gate[:, k * E:(k + 1) * E], gate_sb[:, k * P:(k + 1) * P],
                                           ident[0:E, 0:E])
            last.then_inc(pre_pe, 1)
            pe.wait_ge(onehot_ok, 1)
            for k in range(K):
                last = nc.tensor.matmul(ps_exp[0][:, k * B:(k + 1) * B], bias_sb[:, k * P:(k + 1) * P], onehot_c[:],
                                        start=True, stop=True)
            last.then_inc(pre_pe, 1)

            def turn(u, j):
                pe.wait_ge(x_in[j], (u // RING + 1) * 16 if isinstance(u, int) else (u - j) * (16 // RING) + 16)
                if is_past(u, 1):
                    pe.wait_ge(xlo_ok, u)
                for k in range(K):
                    last = nc.tensor.transpose(ps_turn[:, k, :], x_sb[:, j, k * P:(k + 1) * P], ident[:])
                last.then_inc(turned, 1)

            def cond(u, j):
                s = j % 2
                pe.wait_ge(xlo_ok, u + 1)
                pe.wait_ge(wlo_ok, u + 1)
                if is_past(u, 1):
                    pe.wait_ge(hf_ok, u)
                for b in range(BT):
                    for o in range(K):
                        n = 0
                        for k in range(K):
                            for w in (w_hi, w_lo):
                                n += 1
                                last = nc.tensor.matmul(ps_cond[:, o, b].rearrange("p s t -> p (s t)"),
                                                        w[:, s, b, k, o * P:(o + 1) * P],
                                                        xt[:, s, k, b].rearrange("p s t -> p (s t)"),
                                                        start=(n == 1), stop=(n == 2 * K))
                last.then_inc(conded, 1)

            turn(0, 0)
            turn(1, 1)
            cond(0, 0)

            def step(u, j):
                s = j % 2
                pe.wait_ge(hlo_ok, u + 1)
                if is_past(u, 1):
                    pe.wait_ge(lg2_ok, u)
                else:
                    pe.wait_ge(gatelo_ok, 1)
                    pe.wait_ge(pre_copied, 2)
                n = 0
                for k in range(K):
                    for h in (h_hi, h_lo):
                        n += 1
                        last = nc.tensor.matmul(ps_gate[:, 0:2 * E], h[:, s, k, :],
                                                gate_hl[:, k].rearrange("p s e -> p (s e)"),
                                                start=(n == 1), stop=(n == 2 * K))
                last.then_inc(gated, 1)
                if is_within(u, 1):
                    cond(u + 1, (j + 1) % RING)
                if is_within(u, 2):
                    turn(u + 2, (j + 2) % RING)
                for bank in range(BANKS):
                    if is_past(u, 1):
                        pe.wait_ge(added, (u - 1) * E + 2 * bank + 2)
                    else:
                        pe.wait_ge(welo_ok, bank + 1)
                    cols = slice(bank * M, (bank + 1) * M)
                    n = 0
                    for k in range(K):
                        for h, w in ((h_hi, we_hi), (h_hi, we_lo), (h_lo, we_hi)):
                            n += 1
                            last = nc.tensor.matmul(ps_exp[bank][:], h[:, s, k, :], w[:, k, cols],
                                                    start=(n == 1), stop=(n == 3 * K))
                    last.then_inc(banked, 1)

            tiles(pe, step)


def kernel(x, itok_B_0_30, L0_cond_W, L0_cond_b, L0_ffn_gate_w, L0_ffn_We):
    import numpy as np
    import concourse.bacc as bacc
    from concourse.bass_utils import run_bass_kernel_spmd as run

    nc = bacc.Bacc("TRN2", target_bir_lowering=False, num_devices=1)
    arrays, args = {}, []
    for name, a in (("x", x), ("cat", itok_B_0_30), ("W", L0_cond_W), ("bias", L0_cond_b),
                    ("gate", L0_ffn_gate_w), ("We", L0_ffn_We)):
        a = np.ascontiguousarray(a)
        arrays[name + "_dram"] = a
        args.append(nc.dram_tensor(name + "_dram", a.shape, mybir.dt.from_np(a.dtype), kind="ExternalInput").ap())
    out = nc.dram_tensor("out_dram", x.shape, F32, kind="ExternalOutput").ap()
    build(nc, *args, out)
    r = run(nc, [arrays], core_ids=[0])
    return r.results[0]["out_dram"]
```

```python
from contextlib import ExitStack

import concourse.bass as bass
from concourse import mybir

F32 = mybir.dt.float32
F32R = mybir.dt.float32r
I32 = mybir.dt.int32
U32 = mybir.dt.uint32
ALU = mybir.AluOpType
ACT = mybir.ActivationFunctionType

P = 128
RING = 4


def build(nc, x, cat, W, bias, gate, We, out):
    B, T, D = x.shape
    C = W.shape[0]
    E = We.shape[0]
    K = D // P
    BT = P // T
    TILES = B * T // P
    G = 2 * E
    starts = [0] + [G + e * D for e in range(1, E, 2)] + [G + E * D]
    BANKS = len(starts) - 1
    EXPERTS = [[0]] + [[e, e + 1] for e in range(1, E - 1, 2)] + [[E - 1]]
    assert K * P == D and BT * T == P and TILES % RING == 0 and 2 * D == 512 and E % 2 == 0

    x_t = x.rearrange("b t d -> (b t) d").rearrange("(n p) d -> n p d", p=P)
    out_t = out.rearrange("b t d -> (b t) d").rearrange("(n p) d -> n p d", p=P)

    ctx = ExitStack()
    with ctx:
        def sb(name, shape, dt=F32):
            return ctx.enter_context(nc.sbuf_tensor(name, shape, dt))

        def pb(name, shape, dt=F32):
            return ctx.enter_context(nc.psum_tensor(name, shape, dt))

        def sem(name):
            return ctx.enter_context(nc.semaphore(name))

        ident = sb("ident", [P, P])
        iota_e = sb("iota_e", [P, E])
        iota_c = sb("iota_c", [C, 1])
        cats = sb("cats", [1, B], I32)
        cats_all = sb("cats_all", [C, B], I32)
        cats_f = sb("cats_f", [C, B])
        onehot_c = sb("onehot_c", [C, B])
        bias_sb = sb("bias_sb", [C, D])
        bias_t = sb("bias_t", [P, K, B])
        gate_sb = sb("gate_sb", [E, D])
        gate_f = sb("gate_f", [P, K, E])
        we_f = sb("we_f", [P, K, E * D])
        we_hi = sb("we_hi", [P, K, G + E * D], F32R)
        we_lo = sb("we_lo", [P, K, E * D], F32R)
        x_sb = sb("x_sb", [P, RING, D])
        x_keep = sb("x_keep", [P, RING, D])
        w_sb = sb("w_sb", [P, RING, BT, K, D])
        w_hi = sb("w_hi", [P, RING, BT, K, D], F32R)
        w_lo = sb("w_lo", [P, RING, BT, K, D], F32R)
        xt = sb("xt", [P, RING, K, BT, 2, T], F32R)
        h_low = sb("h_low", [P, RING, K, BT, T])
        h_bias = sb("h_bias", [P, RING, K, BT, T])
        h_f = sb("h_f", [P, RING, K, BT, T])
        h_hi = sb("h_hi", [P, RING, K, P], F32R)
        h_lo = sb("h_lo", [P, RING, K, P], F32R)
        lg2 = sb("lg2", [P, RING, 2, E])
        lg = sb("lg", [P, RING, E])
        top = sb("top", [P, RING, 8])
        topi = sb("topi", [P, RING, 8], U32)
        topf = sb("topf", [P, RING, 2])
        ex = sb("ex", [P, RING, 1])
        den = sb("den", [P, RING, 1])
        w1 = sb("w1", [P, RING, 1])
        w2 = sb("w2", [P, RING, 1])
        wt1 = sb("wt1", [P, RING, E])
        wt2 = sb("wt2", [P, RING, E])
        wt = sb("wt", [P, RING, E])
        acc = sb("acc", [P, RING, 2, D])

        ps_turn = pb("ps_turn", [P, K, P])
        ps_cond = pb("ps_cond", [P, K, BT, 2, T])
        ps_set = pb("ps_set", [P, 512])
        ps_exp = [pb(f"ps_exp{j}", [P, 512]) for j in range(BANKS)]

        cats_in = sem("cats_in")
        small_in = sem("small_in")
        x_in = [sem(f"x_in{j}") for j in range(RING)]
        w_in = [sem(f"w_in{j}") for j in range(RING)]
        we_in = [sem(f"we_in{j}") for j in range(BANKS)]
        filled = sem("filled")
        ident_ok = sem("ident_ok")
        catsf_ok = sem("catsf_ok")
        onehot_ok = sem("onehot_ok")
        pre_pe = sem("pre_pe")
        pre_copied = sem("pre_copied")
        gatehi_ok = sem("gatehi_ok")
        gatelo_ok = sem("gatelo_ok")
        wehi_ok = sem("wehi_ok")
        welo_ok = sem("welo_ok")
        kept = sem("kept")
        turned = sem("turned")
        xhi_ok = sem("xhi_ok")
        xlo_ok = sem("xlo_ok")
        whi_ok = sem("whi_ok")
        wlo_ok = sem("wlo_ok")
        conded = sem("conded")
        hlow_ok = sem("hlow_ok")
        hbias_ok = sem("hbias_ok")
        hf_ok = sem("hf_ok")
        hhi_ok = sem("hhi_ok")
        hlo_ok = sem("hlo_ok")
        lg2_ok = sem("lg2_ok")
        lg_ok = sem("lg_ok")
        top_ok = sem("top_ok")
        topi_ok = sem("topi_ok")
        topf_ok = sem("topf_ok")
        ex_ok = sem("ex_ok")
        den_ok = sem("den_ok")
        w1_ok = sem("w1_ok")
        w2_ok = sem("w2_ok")
        wt12_ok = sem("wt12_ok")
        wt_ok = sem("wt_ok")
        gated = sem("gated")
        banked = sem("banked")
        added = sem("added")
        stored = [sem(f"stored{j}") for j in range(RING)]

        block = ctx.enter_context(nc.Block())

        def tiles(eng, step, tail=RING):
            for j in range(RING):
                step(j, j)
            with eng.Fori(1, (TILES - tail) // RING) as i:
                for j in range(RING):
                    step(i * RING + j, j)
            for u in range(TILES - tail, TILES):
                step(u, u % RING)

        def is_past(u, n):
            return not isinstance(u, int) or u >= n

        def is_within(u, n):
            return not isinstance(u, int) or u + n < TILES

        @block.sync
        def _(sp):
            sp.dma_start(cats[:], cat.rearrange("(a b) -> a b", a=1)).then_inc(cats_in, 16)
            sp.dma_start(x_sb[:, 0, :], x_t[0]).then_inc(x_in[0], 16)

            def load_w(u, j):
                for b in range(BT):
                    c = sp.value_load(cats[0:1, bass.ds(u * BT + b, 1)], min_val=0, max_val=C - 1)
                    sp.dma_start(w_sb[:, j, b], W[bass.ds(c, 1)].rearrange("a (k p) o -> p (a k) o", p=P)
                                 ).then_inc(w_in[j], 16)

            sp.wait_ge(cats_in, 16)
            load_w(0, 0)
            sp.dma_start(x_sb[:, 1, :], x_t[1]).then_inc(x_in[1], 16)
            load_w(1, 1)
            sp.dma_start(x_sb[:, 2, :], x_t[2]).then_inc(x_in[2], 16)
            for n in range(BANKS):
                for e in EXPERTS[n]:
                    sp.dma_start(we_f[:, :, e * D:(e + 1) * D], We[e].rearrange("(k p) m -> p k m", p=P)
                                 ).then_inc(we_in[n], 16)
                if n in (1, 3):
                    load_w(2 + n // 2, 2 + n // 2)
            sp.dma_start(x_sb[:, 3, :], x_t[3]).then_inc(x_in[3], 16)

            def next_w(u, j):
                sp.wait_ge(whi_ok, u + 1)
                sp.wait_ge(wlo_ok, u + 1)
                load_w(u + RING, j)

            for j in range(RING):
                next_w(j, j)

            def next_x(u, j):
                sp.wait_ge(turned, u + 1)
                sp.wait_ge(kept, u + 1)
                sp.dma_start(x_sb[:, j, :], x_t[bass.ds(u + RING, 1)].rearrange("a p d -> p (a d)")
                             ).then_inc(x_in[j], 16)

            for j in range(3):
                next_x(j, j)

            def step(u, j):
                if is_within(u, 2 * RING):
                    next_w(u + RING, j)
                if is_within(u, 3 + RING):
                    next_x(u + 3, (j + 3) % RING)
                sp.wait_ge(added, (u + 1) * E)
                sp.dma_start(out_t[bass.ds(u, 1)].rearrange("a p d -> p (a d)"), acc[:, j, 1, :]
                             ).then_inc(stored[j], 16)

            tiles(sp, step, tail=2 * RING)
            for j in range(RING):
                sp.wait_ge(stored[j], 16 * TILES // RING)

        @block.gpsimd
        def _(pool):
            nc.gpsimd.memset(ident[:], 0.0).then_inc(filled, 1)
            nc.gpsimd.iota(iota_e[:], pattern=[[1, E]], base=0, channel_multiplier=0,
                           allow_small_or_imprecise_dtypes=True).then_inc(filled, 1)
            nc.gpsimd.iota(iota_c[:], pattern=[[0, 1]], base=0, channel_multiplier=1,
                           allow_small_or_imprecise_dtypes=True).then_inc(filled, 1)
            pool.wait_ge(filled, 3)
            nc.gpsimd.affine_select(out=ident[:], in_=ident[:], compare_op=ALU.not_equal, fill=1.0, base=0,
                                    pattern=[[-1, P]], channel_multiplier=1).then_inc(ident_ok, 1)

            def split_w(u, j):
                pool.wait_ge(whi_ok, u + 1)
                if is_past(u, RING):
                    pool.wait_ge(conded, u - RING + 1)
                nc.gpsimd.tensor_tensor(w_lo[:, j], w_sb[:, j], w_hi[:, j].bitcast(F32),
                                        ALU.subtract).then_inc(wlo_ok, 1)

            def add_bias(u, j):
                pool.wait_ge(hlow_ok, u + 1)
                if not is_past(u, 1):
                    pool.wait_ge(pre_copied, 2)
                nc.gpsimd.tensor_tensor(h_bias[:, j], h_low[:, j],
                                        bias_t[:, :, bass.ds(u * BT, BT)].unsqueeze(3).to_broadcast([P, K, BT, T]),
                                        ALU.add).then_inc(hbias_ok, 1)

            def split_h(u, j):
                pool.wait_ge(hhi_ok, u + 1)
                if is_past(u, RING):
                    pool.wait_ge(banked, (u - RING + 1) * (BANKS - 1))
                nc.gpsimd.tensor_tensor(h_lo[:, j], h_f[:, j].rearrange("p k b t -> p k (b t)"),
                                        h_hi[:, j].bitcast(F32), ALU.subtract).then_inc(hlo_ok, 1)

            add_bias(0, 0)
            split_h(0, 0)
            add_bias(1, 1)
            split_h(1, 1)
            pool.wait_ge(wlo_ok, 2)
            split_w(2, 2)
            split_w(3, 3)

            def step(u, j):
                if is_within(u, 2):
                    add_bias(u + 2, (j + 2) % RING)
                    split_h(u + 2, (j + 2) % RING)
                if is_within(u, 4):
                    split_w(u + 4, j)

            tiles(pool, step)

        @block.scalar
        def _(act):
            act.dma_start(cats_all[:], cat.partition_broadcast(C)).then_inc(small_in, 16)
            act.dma_start(bias_sb[:], bias).then_inc(small_in, 16)
            act.dma_start(gate_sb[:], gate).then_inc(small_in, 16)

            def turn_hi(u, j):
                act.wait_ge(turned, u + 1)
                if is_past(u, RING):
                    act.wait_ge(conded, u - RING + 1)
                nc.scalar.activation(xt[:, j, :, :, 0, :], ps_turn[:].rearrange("p k (b t) -> p k b t", b=BT),
                                     ACT.Copy).then_inc(xhi_ok, 1)

            def keep_x(u, j):
                act.wait_ge(x_in[j], (u // RING + 1) * 16 if isinstance(u, int) else (u - j) * (16 // RING) + 16)
                if is_past(u, RING):
                    act.wait_ge(added, (u - RING) * E + 1)
                nc.scalar.activation(x_keep[:, j, :], x_sb[:, j, :], ACT.Copy).then_inc(kept, 1)

            def w_high(u, j):
                act.wait_ge(w_in[j], (u // RING + 1) * 16 * BT if isinstance(u, int) else (u - j) * (16 * BT // RING) + 16 * BT)
                if is_past(u, RING):
                    act.wait_ge(conded, u - RING + 1)
                    act.wait_ge(wlo_ok, u - RING + 1)
                nc.scalar.activation(w_hi[:, j], w_sb[:, j], ACT.Copy).then_inc(whi_ok, 1)

            def cond_low(u, j):
                act.wait_ge(conded, u + 1)
                if is_past(u, RING):
                    act.wait_ge(hbias_ok, u - RING + 1)
                nc.scalar.activation(h_low[:, j], ps_cond[:, :, :, 1, :], ACT.Copy).then_inc(hlow_ok, 1)

            def h_high(u, j):
                act.wait_ge(hf_ok, u + 1)
                if is_past(u, RING):
                    act.wait_ge(banked, (u - RING + 1) * (BANKS - 1))
                    act.wait_ge(hlo_ok, u - RING + 1)
                nc.scalar.activation(h_hi[:, j], h_f[:, j].rearrange("p k b t -> p k (b t)"),
                                     ACT.Copy).then_inc(hhi_ok, 1)

            def gate_copy(u, j):
                act.wait_ge(gated, u + 1)
                if is_past(u, RING):
                    act.wait_ge(lg_ok, u - RING + 1)
                nc.scalar.activation(lg2[:, j], ps_exp[0][:, 0:G].rearrange("p (s e) -> p s e", s=2),
                                     ACT.Copy).then_inc(lg2_ok, 1)

            def exp_second(u, j):
                act.wait_ge(top_ok, u + 1)
                if is_past(u, RING):
                    act.wait_ge(w2_ok, u - RING + 1)
                nc.scalar.activation(ex[:, j], top[:, j, 0:1], ACT.Exp, bias=top[:, j, 1:2],
                                     scale=-1.0).then_inc(ex_ok, 1)

            turn_hi(0, 0)
            w_high(0, 0)
            turn_hi(1, 1)
            act.wait_ge(pre_pe, 1)
            nc.scalar.activation(gate_f[:], ps_set[:, 0:K * E].rearrange("p (k e) -> p k e", k=K),
                                 ACT.Copy).then_inc(pre_copied, 1)
            act.wait_ge(pre_copied, 1)
            nc.scalar.activation(we_hi[:, :, 0:E], gate_f[:], ACT.Copy).then_inc(gatehi_ok, 1)
            act.wait_ge(pre_pe, 2)
            nc.scalar.activation(bias_t[:], ps_exp[0][:, 0:K * B].rearrange("p (k b) -> p k b", k=K),
                                 ACT.Copy).then_inc(pre_copied, 1)
            w_high(1, 1)
            cond_low(0, 0)
            turn_hi(2, 2)

            def we_high(n):
                act.wait_ge(we_in[n], 16 * len(EXPERTS[n]))
                cols = slice(EXPERTS[n][0] * D, (EXPERTS[n][-1] + 1) * D)
                nc.scalar.activation(we_hi[:, :, G + cols.start:G + cols.stop], we_f[:, :, cols],
                                     ACT.Copy).then_inc(wehi_ok, 1)

            we_high(0)
            h_high(0, 0)
            cond_low(1, 1)
            we_high(1)
            w_high(2, 2)
            h_high(1, 1)
            we_high(2)
            we_high(3)
            we_high(4)
            gate_copy(0, 0)
            exp_second(0, 0)
            w_high(3, 3)
            for n in range(3):
                keep_x(n, n)

            def step(u, j):
                if is_within(u, 3):
                    turn_hi(u + 3, (j + 3) % RING)
                    keep_x(u + 3, (j + 3) % RING)
                if is_within(u, 2):
                    cond_low(u + 2, (j + 2) % RING)
                    h_high(u + 2, (j + 2) % RING)
                if is_within(u, 1):
                    gate_copy(u + 1, (j + 1) % RING)
                    exp_second(u + 1, (j + 1) % RING)
                if is_within(u, 4):
                    w_high(u + 4, j)

            tiles(act, step)

        @block.vector
        def _(dve):
            dve.wait_ge(small_in, 16 * 3)
            nc.vector.tensor_copy(cats_f[:], cats_all[:]).then_inc(catsf_ok, 1)
            dve.wait_ge(catsf_ok, 1)
            dve.wait_ge(filled, 3)
            nc.vector.tensor_scalar(onehot_c[:], cats_f[:], iota_c[:, 0:1], None, ALU.is_equal).then_inc(onehot_ok, 1)
            def turn_lo(u, j):
                dve.wait_ge(xhi_ok, u + 1)
                nc.vector.tensor_tensor(xt[:, j, :, :, 1, :], ps_turn[:].rearrange("p k (b t) -> p k b t", b=BT),
                                        xt[:, j, :, :, 0, :].bitcast(F32), ALU.subtract).then_inc(xlo_ok, 1)

            def cond_sum(u, j):
                dve.wait_ge(hbias_ok, u + 1)
                if is_past(u, RING):
                    dve.wait_ge(hlo_ok, u - RING + 1)
                nc.vector.tensor_tensor(h_f[:, j], ps_cond[:, :, :, 0, :], h_bias[:, j],
                                        ALU.add).then_inc(hf_ok, 1)

            def logits(u, j):
                if is_past(u, RING):
                    dve.wait_ge(ex_ok, u - RING + 1)
                dve.wait_ge(lg2_ok, u + 1)
                nc.vector.tensor_tensor(lg[:, j], lg2[:, j, 0], lg2[:, j, 1], ALU.add).then_inc(lg_ok, 1)

            def top_values(u, j):
                dve.wait_ge(filled, 3)
                dve.wait_ge(lg_ok, u + 1)
                nc.vector.max(top[:, j], lg[:, j]).then_inc(top_ok, 1)

            def top_experts(u, j):
                dve.wait_ge(filled, 3)
                dve.wait_ge(top_ok, u + 1)
                nc.vector.max_index(topi[:, j], top[:, j], lg[:, j]).then_inc(topi_ok, 1)

            def top_as_float(u, j):
                dve.wait_ge(topi_ok, u + 1)
                nc.vector.tensor_copy(topf[:, j], topi[:, j, 0:2]).then_inc(topf_ok, 1)

            def denominator(u, j):
                dve.wait_ge(ex_ok, u + 1)
                nc.vector.tensor_scalar_add(den[:, j], ex[:, j], 1.0).then_inc(den_ok, 1)

            def first_weight(u, j):
                dve.wait_ge(den_ok, u + 1)
                nc.vector.reciprocal(w1[:, j], den[:, j]).then_inc(w1_ok, 1)

            def second_weight(u, j):
                dve.wait_ge(w1_ok, u + 1)
                nc.vector.tensor_tensor(w2[:, j], ex[:, j], w1[:, j], ALU.mult).then_inc(w2_ok, 1)

            def spread_weights(u, j):
                dve.wait_ge(w2_ok, u + 1)
                dve.wait_ge(topf_ok, u + 1)
                for wtn, wn, n in ((wt1, w1, 0), (wt2, w2, 1)):
                    nc.vector.tensor_scalar(wtn[:, j], iota_e[:], topf[:, j, n:n + 1], wn[:, j],
                                            ALU.is_equal, ALU.mult).then_inc(wt12_ok, 1)

            def all_weights(u, j):
                dve.wait_ge(wt12_ok, 2 * (u + 1))
                nc.vector.tensor_tensor(wt[:, j], wt1[:, j], wt2[:, j], ALU.add).then_inc(wt_ok, 1)

            def add_expert(u, j, e):
                if e == 0:
                    dve.wait_ge(wt_ok, u + 1)
                    dve.wait_ge(kept, u + 1)
                    if is_past(u, RING):
                        dve.wait_ge(stored[j], (u - j) * (16 // RING))
                bank = (e + 1) // 2
                if e == 0:
                    dve.wait_ge(gated, u + 1)
                elif e == EXPERTS[bank][0]:
                    dve.wait_ge(banked, u * (BANKS - 1) + bank)
                if e:
                    dve.wait_ge(added, u * E + e)
                at = G if e == 0 else (e - EXPERTS[bank][0]) * D
                before = acc[:, j, (e + 1) % 2, :] if e else x_keep[:, j, :]
                nc.vector.scalar_tensor_tensor(
                    out=acc[:, j, e % 2, :], in0=ps_exp[bank][:, at:at + D],
                    scalar=wt[:, j, e:e + 1], in1=before, op0=ALU.mult, op1=ALU.add).then_inc(added, 1)

            def we_low(n):
                dve.wait_ge(wehi_ok, n + 1)
                cols = slice(EXPERTS[n][0] * D, (EXPERTS[n][-1] + 1) * D)
                nc.vector.tensor_tensor(we_lo[:, :, cols], we_f[:, :, cols],
                                        we_hi[:, :, G + cols.start:G + cols.stop].bitcast(F32),
                                        ALU.subtract).then_inc(welo_ok, 1)

            def w_low(u, j):
                dve.wait_ge(whi_ok, u + 1)
                nc.vector.tensor_tensor(w_lo[:, j], w_sb[:, j], w_hi[:, j].bitcast(F32),
                                        ALU.subtract).then_inc(wlo_ok, 1)

            turn_lo(0, 0)
            w_low(0, 0)
            dve.wait_ge(gatehi_ok, 1)
            nc.vector.tensor_tensor(we_hi[:, :, E:G], gate_f[:], we_hi[:, :, 0:E].bitcast(F32),
                                    ALU.subtract).then_inc(gatelo_ok, 1)
            turn_lo(1, 1)
            w_low(1, 1)
            cond_sum(0, 0)
            turn_lo(2, 2)
            we_low(0)
            cond_sum(1, 1)
            for n in range(1, BANKS):
                we_low(n)
            for part in (logits, top_values, top_experts, top_as_float,
                         denominator, first_weight, second_weight, spread_weights, all_weights):
                part(0, 0)

            def step(u, j):
                def ahead(part):
                    if is_within(u, 1):
                        part(u + 1, (j + 1) % RING)

                add_expert(u, j, 0)
                if is_within(u, 3):
                    turn_lo(u + 3, (j + 3) % RING)
                add_expert(u, j, 1)
                add_expert(u, j, 2)
                if is_within(u, 2):
                    cond_sum(u + 2, (j + 2) % RING)
                add_expert(u, j, 3)
                ahead(logits)
                add_expert(u, j, 4)
                ahead(top_values)
                ahead(top_experts)
                add_expert(u, j, 5)
                ahead(top_as_float)
                ahead(denominator)
                add_expert(u, j, 6)
                ahead(first_weight)
                add_expert(u, j, 7)
                ahead(second_weight)
                ahead(spread_weights)
                ahead(all_weights)

            tiles(dve, step)

        @block.tensor
        def _(pe):
            def turn(u, j):
                pe.wait_ge(x_in[j], (u // RING + 1) * 16 if isinstance(u, int) else (u - j) * (16 // RING) + 16)
                if is_past(u, 1):
                    pe.wait_ge(xlo_ok, u)
                for k in range(K):
                    last = nc.tensor.transpose(ps_turn[:, k, :], x_sb[:, j, k * P:(k + 1) * P], ident[:])
                last.then_inc(turned, 1)

            def cond(u, j, b):
                if b == 0:
                    pe.wait_ge(xlo_ok, u + 1)
                    pe.wait_ge(wlo_ok, u + 1)
                    if is_past(u, 1):
                        pe.wait_ge(hf_ok, u)
                for o in range(K):
                    n = 0
                    for k in range(K):
                        for w in (w_hi, w_lo):
                            n += 1
                            last = nc.tensor.matmul(ps_cond[:, o, b].rearrange("p s t -> p (s t)"),
                                                    w[:, j, b, k, o * P:(o + 1) * P],
                                                    xt[:, j, k, b].rearrange("p s t -> p (s t)"),
                                                    start=(n == 1), stop=(n == 2 * K))
                if b == BT - 1:
                    last.then_inc(conded, 1)

            def experts(u, j, bank):
                if bank == 0:
                    pe.wait_ge(hlo_ok, u + 1)
                    if not is_past(u, 1):
                        pe.wait_ge(gatelo_ok, 1)
                if is_past(u, 1):
                    pe.wait_ge(added, (u - 1) * E + EXPERTS[bank][-1] + 1)
                else:
                    pe.wait_ge(welo_ok, bank + 1)
                hi = we_hi[:, :, starts[bank]:starts[bank + 1]] if bank else we_hi[:, :, 0:G + D]
                lo = we_lo[:, :, EXPERTS[bank][0] * D:(EXPERTS[bank][-1] + 1) * D]
                width = hi.shape[-1]
                low_at = width - lo.shape[-1]
                n = 0
                for k in range(K):
                    for h, w, at in ((h_hi, hi, 0), (h_hi, lo, low_at), (h_lo, hi, 0)):
                        n += 1
                        last = nc.tensor.matmul(ps_exp[bank][:, at:width], h[:, j, k, :], w[:, k, :],
                                                start=(n == 1), stop=(n == 3 * K))
                last.then_inc(banked if bank else gated, 1)

            pe.wait_ge(ident_ok, 1)
            turn(0, 0)
            pe.wait_ge(small_in, 16 * 3)
            for k in range(K):
                last = nc.tensor.transpose(ps_set[:, k * E:(k + 1) * E], gate_sb[:, k * P:(k + 1) * P],
                                           ident[0:E, 0:E])
            last.then_inc(pre_pe, 1)
            pe.wait_ge(onehot_ok, 1)
            for k in range(K):
                last = nc.tensor.matmul(ps_exp[0][:, k * B:(k + 1) * B], bias_sb[:, k * P:(k + 1) * P], onehot_c[:],
                                        start=True, stop=True)
            last.then_inc(pre_pe, 1)
            turn(1, 1)
            for b in range(BT):
                cond(0, 0, b)
            turn(2, 2)
            for b in range(BT):
                cond(1, 1, b)
            experts(0, 0, 0)

            def step(u, j):
                if is_within(u, 3):
                    turn(u + 3, (j + 3) % RING)
                if is_within(u, 2):
                    cond(u + 2, (j + 2) % RING, 0)
                experts(u, j, 1)
                if is_within(u, 2):
                    cond(u + 2, (j + 2) % RING, 1)
                experts(u, j, 2)
                if is_within(u, 1):
                    experts(u + 1, (j + 1) % RING, 0)
                experts(u, j, 3)
                experts(u, j, 4)

            tiles(pe, step)


def kernel(x, itok_B_0_30, L0_cond_W, L0_cond_b, L0_ffn_gate_w, L0_ffn_We):
    import numpy as np
    import concourse.bacc as bacc
    from concourse.bass_utils import run_bass_kernel_spmd as run

    nc = bacc.Bacc("TRN2", target_bir_lowering=False, num_devices=1)
    arrays, args = {}, []
    for name, a in (("x", x), ("cat", itok_B_0_30), ("W", L0_cond_W), ("bias", L0_cond_b),
                    ("gate", L0_ffn_gate_w), ("We", L0_ffn_We)):
        a = np.ascontiguousarray(a)
        arrays[name + "_dram"] = a
        args.append(nc.dram_tensor(name + "_dram", a.shape, mybir.dt.from_np(a.dtype), kind="ExternalInput").ap())
    out = nc.dram_tensor("out_dram", x.shape, F32, kind="ExternalOutput").ap()
    build(nc, *args, out)
    r = run(nc, [arrays], core_ids=[0])
    return r.results[0]["out_dram"]
```

```python
from contextlib import ExitStack

import concourse.bass as bass
from concourse import mybir

F32 = mybir.dt.float32
F32R = mybir.dt.float32r
BF16 = mybir.dt.bfloat16
I32 = mybir.dt.int32
U32 = mybir.dt.uint32
ALU = mybir.AluOpType
ACT = mybir.ActivationFunctionType

P = 128
RING = 4


def build(nc, x, cat, W, bias, gate, We, out):
    B, T, D = x.shape
    C = W.shape[0]
    E = We.shape[0]
    K = D // P
    BT = P // T
    TILES = B * T // P
    G = 2 * E
    starts = [0] + [G + e * D for e in range(1, E, 2)] + [G + E * D]
    BANKS = len(starts) - 1
    EXPERTS = [[0]] + [[e, e + 1] for e in range(1, E - 1, 2)] + [[E - 1]]
    assert K * P == D and BT * T == P and TILES % RING == 0 and 2 * D == 512 and E % 2 == 0

    x_t = x.rearrange("b t d -> (b t) d").rearrange("(n p) d -> n p d", p=P)
    out_t = out.rearrange("b t d -> (b t) d").rearrange("(n p) d -> n p d", p=P)

    ctx = ExitStack()
    with ctx:
        def sb(name, shape, dt=F32):
            return ctx.enter_context(nc.sbuf_tensor(name, shape, dt))

        def pb(name, shape, dt=F32):
            return ctx.enter_context(nc.psum_tensor(name, shape, dt))

        def sem(name):
            return ctx.enter_context(nc.semaphore(name))

        ident = sb("ident", [P, P])
        iota_e = sb("iota_e", [P, E])
        iota_c = sb("iota_c", [C, 1])
        cats = sb("cats", [1, B], I32)
        cats_all = sb("cats_all", [C, B], I32)
        cats_f = sb("cats_f", [C, B])
        onehot_c = sb("onehot_c", [C, B])
        bias_sb = sb("bias_sb", [C, D])
        bias_t = sb("bias_t", [P, K, B])
        gate_sb = sb("gate_sb", [E, D])
        gate_f = sb("gate_f", [P, K, E])
        we_f = sb("we_f", [P, K, E * D])
        we_hi = sb("we_hi", [P, K, G + E * D], F32R)
        we_lo = sb("we_lo", [P, K, E * D], F32R)
        x_sb = sb("x_sb", [P, RING, D])
        x_keep = sb("x_keep", [P, RING, D])
        w_sb = sb("w_sb", [P, RING, BT, K, D])
        w_rest = sb("w_rest", [P, RING, BT, K, D])
        w_part = sb("w_part", [P, RING, 3, BT, K, D], BF16)
        x_rest = sb("x_rest", [P, RING, K, P])
        x_part = sb("x_part", [P, RING, 3, K, P], BF16)
        h_f = sb("h_f", [P, RING, K, BT, T])
        h_hi = sb("h_hi", [P, RING, K, P], F32R)
        h_lo = sb("h_lo", [P, RING, K, P], F32R)
        lg2 = sb("lg2", [P, RING, 2, E])
        lg = sb("lg", [P, RING, E])
        top = sb("top", [P, RING, 8])
        topi = sb("topi", [P, RING, 8], U32)
        topf = sb("topf", [P, RING, 2])
        ex = sb("ex", [P, RING, 1])
        den = sb("den", [P, RING, 1])
        w1 = sb("w1", [P, RING, 1])
        w2 = sb("w2", [P, RING, 1])
        wt1 = sb("wt1", [P, RING, E])
        wt2 = sb("wt2", [P, RING, E])
        wt = sb("wt", [P, RING, E])
        acc = sb("acc", [P, RING, 2, D])

        ps_turn = pb("ps_turn", [P, K, P])
        ps_cond = [pb(f"ps_cond{j}", [P, 2, K, BT, T]) for j in range(2)]
        ps_exp = [pb(f"ps_exp{j}", [P, 512]) for j in range(BANKS)]

        cats_in = sem("cats_in")
        small_in = sem("small_in")
        x_in = [sem(f"x_in{j}") for j in range(RING)]
        w_in = [[sem(f"w_in{j}_{b}") for b in range(BT)] for j in range(RING)]
        we_in = [sem(f"we_in{j}") for j in range(BANKS)]
        filled = sem("filled")
        ident_ok = sem("ident_ok")
        catsf_ok = sem("catsf_ok")
        onehot_ok = sem("onehot_ok")
        pre_pe = sem("pre_pe")
        pre_copied = sem("pre_copied")
        gatehi_ok = sem("gatehi_ok")
        gatelo_ok = sem("gatelo_ok")
        wehi_ok = sem("wehi_ok")
        welo_ok = sem("welo_ok")
        kept = sem("kept")
        turned = sem("turned")
        xtop_ok = sem("xtop_ok")
        xrest_ok = sem("xrest_ok")
        xmid_ok = sem("xmid_ok")
        xlow_ok = sem("xlow_ok")
        wtop_ok = sem("wtop_ok")
        wrest_ok = sem("wrest_ok")
        wmid_ok = sem("wmid_ok")
        wlow_ok = sem("wlow_ok")
        conded = sem("conded")
        hf_ok = sem("hf_ok")
        hhi_ok = sem("hhi_ok")
        hlo_ok = sem("hlo_ok")
        lg2_ok = sem("lg2_ok")
        lg_ok = sem("lg_ok")
        top_ok = sem("top_ok")
        topi_ok = sem("topi_ok")
        topf_ok = sem("topf_ok")
        ex_ok = sem("ex_ok")
        den_ok = sem("den_ok")
        w1_ok = sem("w1_ok")
        w2_ok = sem("w2_ok")
        wt12_ok = sem("wt12_ok")
        wt_ok = sem("wt_ok")
        gated = sem("gated")
        banked = sem("banked")
        added = sem("added")
        stored = [sem(f"stored{j}") for j in range(RING)]

        block = ctx.enter_context(nc.Block())

        def tiles(eng, step, tail=RING):
            for j in range(RING):
                step(j, j)
            with eng.Fori(1, (TILES - tail) // RING) as i:
                for j in range(RING):
                    step(i * RING + j, j)
            for u in range(TILES - tail, TILES):
                step(u, u % RING)

        def is_past(u, n):
            return not isinstance(u, int) or u >= n

        def is_within(u, n):
            return not isinstance(u, int) or u + n < TILES

        def loads(u, j):
            return (u // RING + 1) * 16 if isinstance(u, int) else (u - j) * (16 // RING) + 16

        @block.sync
        def _(sp):
            sp.dma_start(cats[:], cat.rearrange("(a b) -> a b", a=1)).then_inc(cats_in, 16)
            sp.dma_start(x_sb[:, 0, :], x_t[0]).then_inc(x_in[0], 16)

            def load_w(u, j):
                for b in range(BT):
                    c = sp.value_load(cats[0:1, bass.ds(u * BT + b, 1)], min_val=0, max_val=C - 1)
                    sp.dma_start(w_sb[:, j, b], W[bass.ds(c, 1)].rearrange("a (k p) o -> p (a k) o", p=P)
                                 ).then_inc(w_in[j][b], 16)

            sp.wait_ge(cats_in, 16)
            load_w(0, 0)
            sp.dma_start(x_sb[:, 1, :], x_t[1]).then_inc(x_in[1], 16)
            load_w(1, 1)
            sp.dma_start(x_sb[:, 2, :], x_t[2]).then_inc(x_in[2], 16)
            for n in range(BANKS):
                for e in EXPERTS[n]:
                    sp.dma_start(we_f[:, :, e * D:(e + 1) * D], We[e].rearrange("(k p) m -> p k m", p=P)
                                 ).then_inc(we_in[n], 16)
                if n == 1:
                    load_w(2, 2)
                if n == 3:
                    sp.dma_start(x_sb[:, 3, :], x_t[3]).then_inc(x_in[3], 16)
            load_w(3, 3)

            def next_w(u, j):
                sp.wait_ge(wtop_ok, (u + 1) * BT)
                sp.wait_ge(wrest_ok, (u + 1) * BT)
                load_w(u + RING, j)

            def next_x(u, j):
                sp.wait_ge(turned, u + 1)
                sp.wait_ge(kept, u + 1)
                sp.dma_start(x_sb[:, j, :], x_t[bass.ds(u + RING, 1)].rearrange("a p d -> p (a d)")
                             ).then_inc(x_in[j], 16)

            for j in range(3):
                next_w(j, j)
                next_x(j, j)
            next_w(3, 3)

            def step(u, j):
                if is_within(u, 3 + RING):
                    next_x(u + 3, (j + 3) % RING)
                if is_within(u, 2 * RING):
                    next_w(u + RING, j)
                sp.wait_ge(added, (u + 1) * E)
                sp.dma_start(out_t[bass.ds(u, 1)].rearrange("a p d -> p (a d)"), acc[:, j, 1, :]
                             ).then_inc(stored[j], 16)

            tiles(sp, step, tail=2 * RING)
            for j in range(RING):
                sp.wait_ge(stored[j], 16 * TILES // RING)

        @block.gpsimd
        def _(pool):
            nc.gpsimd.memset(ident[:], 0.0).then_inc(filled, 1)
            nc.gpsimd.iota(iota_e[:], pattern=[[1, E]], base=0, channel_multiplier=0,
                           allow_small_or_imprecise_dtypes=True).then_inc(filled, 1)
            nc.gpsimd.iota(iota_c[:], pattern=[[0, 1]], base=0, channel_multiplier=1,
                           allow_small_or_imprecise_dtypes=True).then_inc(filled, 1)
            pool.wait_ge(filled, 3)
            nc.gpsimd.affine_select(out=ident[:], in_=ident[:], compare_op=ALU.not_equal, fill=1.0, base=0,
                                    pattern=[[-1, P]], channel_multiplier=1).then_inc(ident_ok, 1)

            def rest_of_w(u, j):
                pool.wait_ge(wtop_ok, (u + 1) * BT)
                if is_past(u, RING):
                    pool.wait_ge(wmid_ok, (u - RING + 1) * BT)
                nc.gpsimd.tensor_tensor(w_rest[:, j], w_sb[:, j], w_part[:, j, 0],
                                        ALU.subtract).then_inc(wrest_ok, BT)

            def low_of_w(u, j):
                pool.wait_ge(wmid_ok, (u + 1) * BT)
                nc.gpsimd.tensor_tensor(w_part[:, j, 2], w_rest[:, j], w_part[:, j, 1],
                                        ALU.subtract).then_inc(wlow_ok, BT)

            def low_of_x(u, j):
                pool.wait_ge(xmid_ok, u + 1)
                nc.gpsimd.tensor_tensor(x_part[:, j, 2], x_rest[:, j], x_part[:, j, 1],
                                        ALU.subtract).then_inc(xlow_ok, 1)

            def split_h(u, j):
                pool.wait_ge(hhi_ok, u + 1)
                if is_past(u, RING):
                    pool.wait_ge(banked, (u - RING + 1) * (BANKS - 1))
                nc.gpsimd.tensor_tensor(h_lo[:, j], h_f[:, j].rearrange("p k b t -> p k (b t)"),
                                        h_hi[:, j].bitcast(F32), ALU.subtract).then_inc(hlo_ok, 1)

            def low_of_batch(u, b):
                pool.wait_ge(wmid_ok, u * BT + b + 1)
                nc.gpsimd.tensor_tensor(w_part[:, u, 2, b], w_rest[:, u, b], w_part[:, u, 1, b],
                                        ALU.subtract).then_inc(wlow_ok, 1)

            low_of_x(0, 0)
            low_of_x(1, 1)
            pool.wait_ge(wlow_ok, BT)
            low_of_batch(1, 0)
            low_of_batch(1, 1)
            split_h(0, 0)
            rest_of_w(2, 2)
            low_of_x(2, 2)
            split_h(1, 1)
            low_of_w(2, 2)
            rest_of_w(3, 3)

            def step(u, j):
                if is_within(u, 3):
                    low_of_x(u + 3, (j + 3) % RING)
                    low_of_w(u + 3, (j + 3) % RING)
                if is_within(u, 2):
                    split_h(u + 2, (j + 2) % RING)
                if is_within(u, 4):
                    rest_of_w(u + 4, j)

            tiles(pool, step)

        @block.scalar
        def _(act):
            act.dma_start(cats_all[:], cat.partition_broadcast(C)).then_inc(small_in, 16)
            act.dma_start(bias_sb[:], bias).then_inc(small_in, 16)
            act.dma_start(gate_sb[:], gate).then_inc(small_in, 16)

            def top_of_x(u, j):
                act.wait_ge(turned, u + 1)
                if is_past(u, RING):
                    act.wait_ge(conded, u - RING + 1)
                nc.scalar.activation(x_part[:, j, 0], ps_turn[:], ACT.Copy).then_inc(xtop_ok, 1)

            def middle_of_x(u, j):
                act.wait_ge(xrest_ok, u + 1)
                nc.scalar.activation(x_part[:, j, 1], x_rest[:, j], ACT.Copy).then_inc(xmid_ok, 1)

            def keep_x(u, j):
                act.wait_ge(x_in[j], loads(u, j))
                if is_past(u, RING):
                    act.wait_ge(added, (u - RING) * E + 1)
                nc.scalar.activation(x_keep[:, j, :], x_sb[:, j, :], ACT.Copy).then_inc(kept, 1)

            def top_of_w(u, j):
                for b in range(BT):
                    act.wait_ge(w_in[j][b], loads(u, j))
                if is_past(u, RING):
                    act.wait_ge(conded, u - RING + 1)
                nc.scalar.activation(w_part[:, j, 0], w_sb[:, j], ACT.Copy).then_inc(wtop_ok, BT)

            def middle_of_w(u, j):
                act.wait_ge(wrest_ok, (u + 1) * BT)
                nc.scalar.activation(w_part[:, j, 1], w_rest[:, j], ACT.Copy).then_inc(wmid_ok, BT)

            def top_of_batch(u, b):
                act.wait_ge(w_in[u][b], loads(u, u))
                nc.scalar.activation(w_part[:, u, 0, b], w_sb[:, u, b], ACT.Copy).then_inc(wtop_ok, 1)

            def middle_of_batch(u, b):
                act.wait_ge(wrest_ok, u * BT + b + 1)
                nc.scalar.activation(w_part[:, u, 1, b], w_rest[:, u, b], ACT.Copy).then_inc(wmid_ok, 1)

            def h_high(u, j):
                act.wait_ge(hf_ok, u + 1)
                if is_past(u, RING):
                    act.wait_ge(banked, (u - RING + 1) * (BANKS - 1))
                    act.wait_ge(hlo_ok, u - RING + 1)
                nc.scalar.activation(h_hi[:, j], h_f[:, j].rearrange("p k b t -> p k (b t)"),
                                     ACT.Copy).then_inc(hhi_ok, 1)

            def gate_copy(u, j):
                act.wait_ge(gated, u + 1)
                if is_past(u, RING):
                    act.wait_ge(lg_ok, u - RING + 1)
                nc.scalar.activation(lg2[:, j], ps_exp[0][:, 0:G].rearrange("p (s e) -> p s e", s=2),
                                     ACT.Copy).then_inc(lg2_ok, 1)

            def exp_second(u, j):
                act.wait_ge(top_ok, u + 1)
                if is_past(u, RING):
                    act.wait_ge(w2_ok, u - RING + 1)
                nc.scalar.activation(ex[:, j], top[:, j, 0:1], ACT.Exp, bias=top[:, j, 1:2],
                                     scale=-1.0).then_inc(ex_ok, 1)

            top_of_x(0, 0)
            act.wait_ge(pre_pe, 1)
            nc.scalar.activation(gate_f[:], ps_exp[1][:, 0:K * E].rearrange("p (k e) -> p k e", k=K),
                                 ACT.Copy).then_inc(pre_copied, 1)
            act.wait_ge(pre_copied, 1)
            nc.scalar.activation(we_hi[:, :, 0:E], gate_f[:], ACT.Copy).then_inc(gatehi_ok, 1)
            middle_of_x(0, 0)
            act.wait_ge(pre_pe, 2)
            nc.scalar.activation(bias_t[:], ps_exp[0][:, 0:K * B].rearrange("p (k b) -> p k b", k=K),
                                 ACT.Copy).then_inc(pre_copied, 1)
            top_of_batch(0, 0)
            top_of_batch(0, 1)
            middle_of_batch(0, 0)
            top_of_x(1, 1)
            middle_of_batch(0, 1)
            top_of_batch(1, 0)
            top_of_batch(1, 1)
            middle_of_x(1, 1)
            middle_of_batch(1, 0)
            middle_of_batch(1, 1)

            def we_high(n):
                act.wait_ge(we_in[n], 16 * len(EXPERTS[n]))
                cols = slice(EXPERTS[n][0] * D, (EXPERTS[n][-1] + 1) * D)
                nc.scalar.activation(we_hi[:, :, G + cols.start:G + cols.stop], we_f[:, :, cols],
                                     ACT.Copy).then_inc(wehi_ok, 1)

            we_high(0)
            top_of_x(2, 2)
            h_high(0, 0)
            we_high(1)
            top_of_w(2, 2)
            middle_of_x(2, 2)
            gate_copy(0, 0)
            we_high(2)
            exp_second(0, 0)
            keep_x(0, 0)
            h_high(1, 1)
            middle_of_w(2, 2)
            we_high(3)
            we_high(4)
            keep_x(1, 1)
            keep_x(2, 2)
            top_of_w(3, 3)

            def step(u, j):
                if is_within(u, 3):
                    top_of_x(u + 3, (j + 3) % RING)
                    middle_of_x(u + 3, (j + 3) % RING)
                    keep_x(u + 3, (j + 3) % RING)
                if is_within(u, 1):
                    gate_copy(u + 1, (j + 1) % RING)
                if is_within(u, 3):
                    middle_of_w(u + 3, (j + 3) % RING)
                if is_within(u, 2):
                    h_high(u + 2, (j + 2) % RING)
                if is_within(u, 1):
                    exp_second(u + 1, (j + 1) % RING)
                if is_within(u, 4):
                    top_of_w(u + 4, j)

            tiles(act, step)

        @block.vector
        def _(dve):
            dve.wait_ge(small_in, 16 * 3)
            nc.vector.tensor_copy(cats_f[:], cats_all[:]).then_inc(catsf_ok, 1)
            dve.wait_ge(catsf_ok, 1)
            dve.wait_ge(filled, 3)
            nc.vector.tensor_scalar(onehot_c[:], cats_f[:], iota_c[:, 0:1], None, ALU.is_equal).then_inc(onehot_ok, 1)

            def rest_of_x(u, j):
                dve.wait_ge(xtop_ok, u + 1)
                nc.vector.tensor_tensor(x_rest[:, j], ps_turn[:], x_part[:, j, 0],
                                        ALU.subtract).then_inc(xrest_ok, 1)

            def cond_sum(u, j):
                dve.wait_ge(conded, u + 1)
                if is_past(u, RING):
                    dve.wait_ge(hlo_ok, u - RING + 1)
                elif not is_past(u, 1):
                    dve.wait_ge(pre_copied, 2)
                nc.vector.tensor_tensor(h_f[:, j], ps_cond[j % 2][:, 0],
                                        bias_t[:, :, bass.ds(u * BT, BT)].unsqueeze(3).to_broadcast([P, K, BT, T]),
                                        ALU.add).then_inc(hf_ok, 1)

            def logits(u, j):
                if is_past(u, RING):
                    dve.wait_ge(ex_ok, u - RING + 1)
                dve.wait_ge(lg2_ok, u + 1)
                nc.vector.tensor_tensor(lg[:, j], lg2[:, j, 0], lg2[:, j, 1], ALU.add).then_inc(lg_ok, 1)

            def top_values(u, j):
                dve.wait_ge(filled, 3)
                dve.wait_ge(lg_ok, u + 1)
                nc.vector.max(top[:, j], lg[:, j]).then_inc(top_ok, 1)

            def top_experts(u, j):
                dve.wait_ge(filled, 3)
                dve.wait_ge(top_ok, u + 1)
                nc.vector.max_index(topi[:, j], top[:, j], lg[:, j]).then_inc(topi_ok, 1)

            def top_as_float(u, j):
                dve.wait_ge(topi_ok, u + 1)
                nc.vector.tensor_copy(topf[:, j], topi[:, j, 0:2]).then_inc(topf_ok, 1)

            def denominator(u, j):
                dve.wait_ge(ex_ok, u + 1)
                nc.vector.tensor_scalar_add(den[:, j], ex[:, j], 1.0).then_inc(den_ok, 1)

            def first_weight(u, j):
                dve.wait_ge(den_ok, u + 1)
                nc.vector.reciprocal(w1[:, j], den[:, j]).then_inc(w1_ok, 1)

            def second_weight(u, j):
                dve.wait_ge(w1_ok, u + 1)
                nc.vector.tensor_tensor(w2[:, j], ex[:, j], w1[:, j], ALU.mult).then_inc(w2_ok, 1)

            def spread_weights(u, j):
                dve.wait_ge(w2_ok, u + 1)
                dve.wait_ge(topf_ok, u + 1)
                for wtn, wn, n in ((wt1, w1, 0), (wt2, w2, 1)):
                    nc.vector.tensor_scalar(wtn[:, j], iota_e[:], topf[:, j, n:n + 1], wn[:, j],
                                            ALU.is_equal, ALU.mult).then_inc(wt12_ok, 1)

            def all_weights(u, j):
                dve.wait_ge(wt12_ok, 2 * (u + 1))
                nc.vector.tensor_tensor(wt[:, j], wt1[:, j], wt2[:, j], ALU.add).then_inc(wt_ok, 1)

            def add_expert(u, j, e):
                if e == 0:
                    dve.wait_ge(wt_ok, u + 1)
                    dve.wait_ge(kept, u + 1)
                    if is_past(u, RING):
                        dve.wait_ge(stored[j], (u - j) * (16 // RING))
                bank = (e + 1) // 2
                if e == 0:
                    dve.wait_ge(gated, u + 1)
                elif e == EXPERTS[bank][0]:
                    dve.wait_ge(banked, u * (BANKS - 1) + bank)
                if e:
                    dve.wait_ge(added, u * E + e)
                at = G if e == 0 else (e - EXPERTS[bank][0]) * D
                before = acc[:, j, (e + 1) % 2, :] if e else x_keep[:, j, :]
                nc.vector.scalar_tensor_tensor(
                    out=acc[:, j, e % 2, :], in0=ps_exp[bank][:, at:at + D],
                    scalar=wt[:, j, e:e + 1], in1=before, op0=ALU.mult, op1=ALU.add).then_inc(added, 1)

            def we_low(n):
                dve.wait_ge(wehi_ok, n + 1)
                cols = slice(EXPERTS[n][0] * D, (EXPERTS[n][-1] + 1) * D)
                nc.vector.tensor_tensor(we_lo[:, :, cols], we_f[:, :, cols],
                                        we_hi[:, :, G + cols.start:G + cols.stop].bitcast(F32),
                                        ALU.subtract).then_inc(welo_ok, 1)

            def rest_of_batch(u, b):
                dve.wait_ge(wtop_ok, u * BT + b + 1)
                nc.vector.tensor_tensor(w_rest[:, u, b], w_sb[:, u, b], w_part[:, u, 0, b],
                                        ALU.subtract).then_inc(wrest_ok, 1)

            def low_of_batch(u, b):
                dve.wait_ge(wmid_ok, u * BT + b + 1)
                nc.vector.tensor_tensor(w_part[:, u, 2, b], w_rest[:, u, b], w_part[:, u, 1, b],
                                        ALU.subtract).then_inc(wlow_ok, 1)

            rest_of_x(0, 0)
            dve.wait_ge(gatehi_ok, 1)
            nc.vector.tensor_tensor(we_hi[:, :, E:G], gate_f[:], we_hi[:, :, 0:E].bitcast(F32),
                                    ALU.subtract).then_inc(gatelo_ok, 1)
            rest_of_batch(0, 0)
            rest_of_batch(0, 1)
            low_of_batch(0, 0)
            rest_of_x(1, 1)
            low_of_batch(0, 1)
            rest_of_batch(1, 0)
            rest_of_batch(1, 1)
            cond_sum(0, 0)
            we_low(0)
            rest_of_x(2, 2)
            we_low(1)
            logits(0, 0)
            cond_sum(1, 1)
            top_values(0, 0)
            top_experts(0, 0)
            we_low(2)
            for part in (top_as_float, denominator, first_weight, second_weight, spread_weights, all_weights):
                part(0, 0)
            we_low(3)
            add_expert(0, 0, 0)
            we_low(4)

            def step(u, j):
                def ahead(part):
                    if is_within(u, 1):
                        part(u + 1, (j + 1) % RING)

                if is_past(u, 1):
                    add_expert(u, j, 0)
                if is_within(u, 3):
                    rest_of_x(u + 3, (j + 3) % RING)
                add_expert(u, j, 1)
                add_expert(u, j, 2)
                add_expert(u, j, 3)
                add_expert(u, j, 4)
                ahead(logits)
                if is_within(u, 2):
                    cond_sum(u + 2, (j + 2) % RING)
                ahead(top_values)
                ahead(top_experts)
                add_expert(u, j, 5)
                ahead(top_as_float)
                ahead(denominator)
                add_expert(u, j, 6)
                ahead(first_weight)
                add_expert(u, j, 7)
                ahead(second_weight)
                ahead(spread_weights)
                ahead(all_weights)

            tiles(dve, step)

        @block.tensor
        def _(pe):
            def turn(u, j):
                pe.wait_ge(x_in[j], loads(u, j))
                if is_past(u, 1):
                    pe.wait_ge(xrest_ok, u)
                for k in range(K):
                    last = nc.tensor.transpose(ps_turn[:, k, :], x_sb[:, j, k * P:(k + 1) * P], ident[:])
                last.then_inc(turned, 1)

            def cond(u, j, b):
                pe.wait_ge(wlow_ok, u * BT + b + 1 if not is_past(u, 2) else (u + 1) * BT)
                if b == 0:
                    pe.wait_ge(xlow_ok, u + 1)
                    if is_past(u, 2):
                        pe.wait_ge(hf_ok, u - 1)
                for o in range(K):
                    n = 0
                    for k in range(K):
                        for wn, xn in ((0, 0), (0, 1), (0, 2), (1, 0), (1, 1), (2, 0)):
                            n += 1
                            last = nc.tensor.matmul(ps_cond[j % 2][:, 0, o, b],
                                                    w_part[:, j, wn, b, k, o * P:(o + 1) * P],
                                                    x_part[:, j, xn, k, b * T:(b + 1) * T],
                                                    start=(n == 1), stop=(n == 6 * K))
                if b == BT - 1:
                    last.then_inc(conded, 1)

            def experts(u, j, bank):
                if bank == 0:
                    pe.wait_ge(hlo_ok, u + 1)
                    if not is_past(u, 1):
                        pe.wait_ge(gatelo_ok, 1)
                if is_past(u, 1):
                    pe.wait_ge(added, (u - 1) * E + EXPERTS[bank][-1] + 1)
                else:
                    pe.wait_ge(welo_ok, bank + 1)
                hi = we_hi[:, :, starts[bank]:starts[bank + 1]] if bank else we_hi[:, :, 0:G + D]
                lo = we_lo[:, :, EXPERTS[bank][0] * D:(EXPERTS[bank][-1] + 1) * D]
                width = hi.shape[-1]
                low_at = width - lo.shape[-1]
                n = 0
                for k in range(K):
                    for h, w, at in ((h_hi, hi, 0), (h_hi, lo, low_at), (h_lo, hi, 0)):
                        n += 1
                        last = nc.tensor.matmul(ps_exp[bank][:, at:width], h[:, j, k, :], w[:, k, :],
                                                start=(n == 1), stop=(n == 3 * K))
                last.then_inc(banked if bank else gated, 1)

            pe.wait_ge(ident_ok, 1)
            turn(0, 0)
            pe.wait_ge(small_in, 16 * 3)
            for k in range(K):
                last = nc.tensor.transpose(ps_exp[1][:, k * E:(k + 1) * E], gate_sb[:, k * P:(k + 1) * P],
                                           ident[0:E, 0:E])
            last.then_inc(pre_pe, 1)
            pe.wait_ge(onehot_ok, 1)
            for k in range(K):
                last = nc.tensor.matmul(ps_exp[0][:, k * B:(k + 1) * B], bias_sb[:, k * P:(k + 1) * P], onehot_c[:],
                                        start=True, stop=True)
            last.then_inc(pre_pe, 1)
            turn(1, 1)
            for b in range(BT):
                cond(0, 0, b)
            turn(2, 2)
            cond(1, 1, 0)
            experts(0, 0, 0)
            cond(1, 1, 1)

            def step(u, j):
                experts(u, j, 1)
                if is_within(u, 3):
                    turn(u + 3, (j + 3) % RING)
                experts(u, j, 2)
                if is_within(u, 2):
                    cond(u + 2, (j + 2) % RING, 0)
                if is_within(u, 1):
                    experts(u + 1, (j + 1) % RING, 0)
                if is_within(u, 2):
                    cond(u + 2, (j + 2) % RING, 1)
                experts(u, j, 3)
                experts(u, j, 4)

            tiles(pe, step)


def kernel(x, itok_B_0_30, L0_cond_W, L0_cond_b, L0_ffn_gate_w, L0_ffn_We):
    import numpy as np
    import concourse.bacc as bacc
    from concourse.bass_utils import run_bass_kernel_spmd as run

    nc = bacc.Bacc("TRN2", target_bir_lowering=False, num_devices=1)
    arrays, args = {}, []
    for name, a in (("x", x), ("cat", itok_B_0_30), ("W", L0_cond_W), ("bias", L0_cond_b),
                    ("gate", L0_ffn_gate_w), ("We", L0_ffn_We)):
        a = np.ascontiguousarray(a)
        arrays[name + "_dram"] = a
        args.append(nc.dram_tensor(name + "_dram", a.shape, mybir.dt.from_np(a.dtype), kind="ExternalInput").ap())
    out = nc.dram_tensor("out_dram", x.shape, F32, kind="ExternalOutput").ap()
    build(nc, *args, out)
    r = run(nc, [arrays], core_ids=[0])
    return r.results[0]["out_dram"]
```
